# Optimizing a Trainium2 kernel written in Bass

```python
import numpy as np
import jax
import jax.numpy as jnp

def _softmax(x, axis=-1):
    return jax.nn.softmax(x, axis=axis)

def _gelu(x):
    return jax.nn.gelu(x, approximate=True)

def _silu(x):
    return jax.nn.silu(x)

def _sigmoid(x):
    return jax.nn.sigmoid(x)

def _layernorm(x, axis=-1, eps=1e-05):
    m = jnp.mean(x, axis=axis, keepdims=True)
    v = jnp.var(x, axis=axis, keepdims=True)
    return (x - m) / jnp.sqrt(v + eps)

def _scatter_add(tgt, idx, src, axis=0):
    return tgt.at[idx].add(src)

def _segment_sum(src, seg, n):
    return jax.ops.segment_sum(src, seg, n)
kernel_name = 'mk_cond_resid_d2_seqx_r4_ebd33e'

def setup_inputs(seed: int=0):
    np.random.seed(seed)
    _w = jnp.asarray

    def _rec_inputs():
        import jax
        import jax.numpy as jnp
        _rk = jax.random.key(seed)
        x = 7.22e-05 + 1 * jax.random.normal(jax.random.fold_in(_rk, 1), (8, 512, 256), jnp.float32)
        _lenS = 512 - jax.random.randint(jax.random.fold_in(_rk, 7), (8,), 0, max(1, 512 // 4) + 1, jnp.int32)
        _lenS2 = 512 - jax.random.randint(jax.random.fold_in(_rk, 8), (8,), 0, max(1, 512 // 4) + 1, jnp.int32)
        cond_8 = jax.random.uniform(jax.random.fold_in(_rk, 11), (8, 8), jnp.float32, 0.0, 0.999837)
        return (x, cond_8)
    x, cond_8 = _rec_inputs()

    def _L0_cond_setup():
        import jax, jax.numpy as jnp
        import numpy as np
        key = jax.random.key(seed)
        k1, k2, k3, k4, k5 = jax.random.split(key, 5)
        B, N, T, O, G = (32, 64, 256, 256, 8)
        x = jax.random.normal(k1, (B, N, T), dtype=jnp.float32)
        y = jax.random.uniform(k2, (B, G), dtype=jnp.float32)
        weight = jax.random.normal(k3, (G, O, T), dtype=jnp.float32) * (1.0 / np.sqrt(T))
        mask = jax.random.uniform(k4, (O, T), dtype=jnp.float32)
        bias = jax.random.normal(k5, (O,), dtype=jnp.float32)
        return {'x': x, 'y': y, 'weight': weight, 'mask': mask, 'bias': bias}
    _L0_cond_all = _L0_cond_setup()
    _L0_cond_in = {k: v for k, v in _L0_cond_all.items() if k in ('weight', 'mask', 'bias')}
    del _L0_cond_all

    def _L1_cond_setup():
        import jax, jax.numpy as jnp
        import numpy as np
        R = 16
        ALPHA = 32.0
        SCALING = ALPHA / R
        key = jax.random.key(seed)
        ks = jax.random.split(key, 6)
        B, T, C, O, E = (16, 375, 256, 256, 8)
        x = jax.random.normal(ks[0], (B, T, C), dtype=jnp.float32)
        w = jax.random.uniform(ks[1], (B, E), dtype=jnp.float32)
        W_base = jax.random.normal(ks[2], (O, C), dtype=jnp.float32) * 0.02
        b_base = jax.random.normal(ks[3], (O,), dtype=jnp.float32) * 0.02
        As = jax.random.normal(ks[4], (E, R, C), dtype=jnp.float32) * 0.02
        Bs = jax.random.normal(ks[5], (E, O, R), dtype=jnp.float32) * 0.02
        return {'x': x, 'w': w, 'W_base': W_base, 'b_base': b_base, 'As': As, 'Bs': Bs}
    _L1_cond_all = _L1_cond_setup()
    _L1_cond_in = {k: v for k, v in _L1_cond_all.items() if k in ('W_base', 'b_base', 'As', 'Bs')}
    del _L1_cond_all
    return {'x': x, 'cond_8': cond_8, 'L0_cond_weight': _L0_cond_in['weight'], 'L0_cond_mask': _L0_cond_in['mask'], 'L0_cond_bias': _L0_cond_in['bias'], 'L1_cond_W_base': _L1_cond_in['W_base'], 'L1_cond_b_base': _L1_cond_in['b_base'], 'L1_cond_As': _L1_cond_in['As'], 'L1_cond_Bs': _L1_cond_in['Bs']}

def reference(x, cond_8, L0_cond_weight, L0_cond_mask, L0_cond_bias, L1_cond_W_base, L1_cond_b_base, L1_cond_As, L1_cond_Bs):
    import jax
    import jax.numpy as jnp

    def _L0_cond_ref(x, y, weight, mask, bias):
        import jax, jax.numpy as jnp
        import numpy as np
        masked_w = weight * mask[None, :, :]
        w_bot = jnp.einsum('bg,got->bot', y, masked_w)
        return jnp.einsum('bnt,bot->bno', x, w_bot) + bias

    def _L1_cond_ref(x, w, W_base, b_base, As, Bs):
        import jax, jax.numpy as jnp
        import numpy as np
        R = 16
        ALPHA = 32.0
        SCALING = ALPHA / R
        out = jnp.einsum('btc,oc->bto', x, W_base) + b_base
        h = jnp.einsum('btc,erc->bter', x, As)
        lora = jnp.einsum('bter,eor,be->bto', h, Bs, w)
        return out + lora * SCALING
    x = x + _L0_cond_ref(x, cond_8, L0_cond_weight, L0_cond_mask, L0_cond_bias)
    x = x + _L1_cond_ref(x, cond_8, L1_cond_W_base, L1_cond_b_base, L1_cond_As, L1_cond_Bs)
    return x

_drawn_inputs = setup_inputs


def setup_inputs(seed=0):
    import zlib

    import numpy as np

    out = dict(_drawn_inputs(seed))
    spreads = {}
    factors = {'L1_cond_b_base': 5.545}
    for name, (base, spread) in spreads.items():
        noise = np.random.default_rng([zlib.crc32(name.encode()), seed]).standard_normal(out[name].shape)
        drawn = base * np.exp(spread * noise) if base else spread * noise
        out[name] = jnp.asarray(drawn.astype(out[name].dtype))
    for name, factor in factors.items():
        out[name] = (out[name] * factor).astype(out[name].dtype)
    return out
```

```python
import concourse.bass as bass
from concourse import mybir
from contextlib import ExitStack


def conditional_residual_kernel(nc: bass.Bass, experts: bass.AP, small: bass.AP, mix: bass.AP,
                                base: bass.AP, mask: bass.AP, xT: bass.AP, outT: bass.AP):
    f32 = mybir.dt.float32
    f32r = mybir.dt.float32r
    ALU = mybir.AluOpType
    ACT = mybir.ActivationFunctionType

    P = 128
    NB, _, XW = xT.shape
    NT = 2
    TOK = XW // NT
    C = base.shape[1] // NT
    NG = 8
    TB = P // NG
    NK = C // TB
    KPD = 4
    NL = NK // KPD
    SLOTS = NL * NT
    SCALING = 32.0 / 16
    OW, OB0, OB1, OAT, OA, OBT = 0, NB, NB + NT, NB + 2 * NT, NB + 2 * NT + C, NB + 2 * NT + 2 * C
    SMALL = small.shape[1]
    assert SMALL == OBT + C

    with ExitStack() as ctx:
        def sb(name, shape, dt=f32):
            return ctx.enter_context(nc.sbuf_tensor(name, shape, dt))

        def pb(name, shape):
            return ctx.enter_context(nc.psum_tensor(name, shape, f32))

        def sem(name):
            return ctx.enter_context(nc.semaphore(name))

        small_sb = sb("small_sb", [P, SMALL])
        cond_er = small_sb[:, OW:OW + NB]
        bias0 = small_sb[:, OB0:OB0 + NT]
        bias1 = small_sb[:, OB1:OB1 + NT]
        A_t = small_sb[:, OAT:OAT + C].rearrange("p (j e) -> p j e", j=NT)
        A_er = small_sb[:, OA:OA + C]
        B_er = small_sb[:, OBT:OBT + C]
        mix_sb = sb("mix_sb", [P, P])
        base_sb = sb("base_sb", [P, NT, C])
        mask_sb = sb("mask_sb", [P, NT, C])
        experts_sb = sb("experts_sb", [P, NK, C])
        x_sb = sb("x_sb", [P, NB, NT, TOK])
        ident = sb("ident", [P, P])
        gate2 = sb("gate2", [P, NB])
        bias0_rep = sb("bias0_rep", [P, NT, NB])
        low_bias = sb("low_bias", [P, NB])
        bias_sb = sb("bias_sb", [P, NT, NB])
        B_hi = sb("B_hi", [P, C], f32r)
        B_lo = sb("B_lo", [P, C], f32r)
        A_hi = sb("A_hi", [P, 2, C], f32r)
        A_lo = sb("A_lo", [P, 2, C], f32r)
        W1 = sb("W1", [P, NB, NT, C])
        W1_hi = sb("W1_hi", [P, NB, NT, C], f32r)
        W1_lo = sb("W1_lo", [P, NB, NT, C], f32r)
        W0 = sb("W0", [P, NB, NT, C])
        W0_hi = sb("W0_hi", [P, 2, NT, C], f32r)
        W0_lo = sb("W0_lo", [P, 2, NT, C], f32r)
        M = sb("M", [P, 2, NT, C])
        M_hi = sb("M_hi", [P, 2, NT, C], f32r)
        M_lo = sb("M_lo", [P, 2, NT, C], f32r)
        x_hi = sb("x_hi", [P, 2, NT, TOK], f32r)
        x_lo = sb("x_lo", [P, 2, NT, TOK], f32r)
        out_sb = sb("out_sb", [P, 2, NT, TOK])

        ps_out = [[pb(f"ps_out{i}{j}", [P, TOK]) for j in range(NT)] for i in range(2)]
        ps_merge = [pb(f"ps_merge{i}", [P, NT, C]) for i in range(2)]
        ps_lora = [pb(f"ps_lora{i}", [P, NT, C]) for i in range(2)]
        ps_mix = ps_out[0]
        ps_bias = ps_out[1][0]

        small_in, mix_in, base_in, mask_in = sem("small_in"), sem("mix_in"), sem("base_in"), sem("mask_in")
        experts_in = [sem(f"experts_in{i}") for i in range(NL)]
        x_in = [sem(f"x_in{b}") for b in range(NB)]
        ident_zero, ident_done = sem("ident_zero"), sem("ident_done")
        gate_done, base_done, rep_done = sem("gate_done"), sem("base_done"), sem("rep_done")
        u_done, low_done, bias_mm, bias_done = sem("u_done"), sem("low_done"), sem("bias_mm"), sem("bias_done")
        bhi_done, blo_done = sem("bhi_done"), sem("blo_done")
        ahi_done, alo_done = sem("ahi_done"), sem("alo_done")
        lora_mm, w1_done, w1hi_done, w1lo_done = sem("lora_mm"), sem("w1_done"), sem("w1hi_done"), sem("w1lo_done")
        mix_mm, w0_done, w0hi_done, w0lo_done = sem("mix_mm"), sem("w0_done"), sem("w0hi_done"), sem("w0lo_done")
        merge_mm, m_done, mhi_done, mlo_done = sem("merge_mm"), sem("m_done"), sem("mhi_done"), sem("mlo_done")
        xhi_done, xlo_done = sem("xhi_done"), sem("xlo_done")
        apply_mm = sem("apply_mm")
        out0_done, out1_done = sem("out0_done"), sem("out1_done")
        stored = [[sem(f"stored{i}{j}") for j in range(NT)] for i in range(2)]

        block = ctx.enter_context(nc.Block())

        @block.sync
        def _(sp):
            sp.dma_start(small_sb[:, :], small).then_inc(small_in, 16)
            sp.dma_start(base_sb[:, :, :], base.rearrange("p (j o) -> p j o", j=NT)).then_inc(base_in, 16)
            sp.dma_start(mix_sb[:, :], mix).then_inc(mix_in, 16)
            for i in range(NL):
                sp.dma_start(experts_sb[:, i * KPD:(i + 1) * KPD, :],
                             experts[:, i * KPD:(i + 1) * KPD, :]).then_inc(experts_in[i], 16)
                if i == 0:
                    sp.dma_start(mask_sb[:, :, :], mask.rearrange("p (j o) -> p j o", j=NT)).then_inc(mask_in, 16)
            for b in range(NB):
                sp.dma_start(x_sb[:, b], xT[b].rearrange("p (j n) -> p j n", j=NT)).then_inc(x_in[b], 16)
            for b in range(NB):
                for j, ready in enumerate((out0_done, out1_done)):
                    sp.wait_ge(ready, b + 1)
                    sp.dma_start(outT[b, j], out_sb[:, b % 2, j, :]).then_inc(stored[b % 2][j], 16)
            for i in range(2):
                for j in range(NT):
                    sp.wait_ge(stored[i][j], 16 * (NB // 2))

        @block.gpsimd
        def _(pool):
            pool.memset(ident[:, :], 0.0).then_inc(ident_zero, 1)
            pool.wait_ge(ident_zero, 1)
            pool.affine_select(out=ident[:, :], in_=ident[:, :], compare_op=ALU.not_equal, fill=1.0,
                               base=0, pattern=[[-1, P]], channel_multiplier=1).then_inc(ident_done, 1)
            pool.wait_ge(bhi_done, 1)
            pool.tensor_tensor(B_lo[:, :], B_er, B_hi[:, :].bitcast(f32), ALU.subtract).then_inc(blo_done, 1)

            def w1_lo(b):
                pool.wait_ge(w1hi_done, b + 1)
                pool.tensor_tensor(W1_lo[:, b], W1[:, b], W1_hi[:, b].bitcast(f32),
                                   ALU.subtract).then_inc(w1lo_done, 1)

            def w0_lo(b):
                pool.wait_ge(w0hi_done, b + 1)
                if b >= 2:
                    pool.wait_ge(merge_mm, b - 1)
                pool.tensor_tensor(W0_lo[:, b % 2], W0[:, b], W0_hi[:, b % 2].bitcast(f32),
                                   ALU.subtract).then_inc(w0lo_done, 1)

            def m_lo(b):
                pool.wait_ge(mhi_done, b + 1)
                if b >= 2:
                    pool.wait_ge(apply_mm, 2 * (b - 1))
                pool.tensor_tensor(M_lo[:, b % 2], M[:, b % 2], M_hi[:, b % 2].bitcast(f32),
                                   ALU.subtract).then_inc(mlo_done, 1)

            for b in range(NB):
                w1_lo(b)
            w0_lo(0)
            w0_lo(1)
            for b in range(NB):
                m_lo(b)
                if b + 2 < NB:
                    w0_lo(b + 2)

        @block.scalar
        def _(act):
            act.wait_ge(small_in, 16)
            nc.scalar.activation(B_hi[:, :], B_er, ACT.Copy).then_inc(bhi_done, 1)
            act.wait_ge(gate_done, 1)

            def a_hi(b):
                if b >= 2:
                    act.wait_ge(lora_mm, b - 1)
                nc.scalar.activation(A_hi[:, b % 2], A_er, ACT.Copy,
                                     scale=gate2[:, b:b + 1]).then_inc(ahi_done, 1)

            def w1_hi(b):
                act.wait_ge(w1_done, b + 1)
                nc.scalar.activation(W1_hi[:, b], W1[:, b], ACT.Copy).then_inc(w1hi_done, 1)

            def w0_hi(b):
                if b == 0:
                    act.wait_ge(w0_done, SLOTS)
                if b >= 2:
                    act.wait_ge(merge_mm, b - 1)
                nc.scalar.activation(W0_hi[:, b % 2], W0[:, b], ACT.Copy).then_inc(w0hi_done, 1)

            def m_hi(b):
                act.wait_ge(m_done, b + 1)
                if b >= 2:
                    act.wait_ge(apply_mm, 2 * (b - 1))
                nc.scalar.activation(M_hi[:, b % 2], M[:, b % 2], ACT.Copy).then_inc(mhi_done, 1)

            def x_hi_(b):
                act.wait_ge(x_in[b], 16)
                if b >= 2:
                    act.wait_ge(apply_mm, 2 * (b - 1))
                nc.scalar.activation(x_hi[:, b % 2], x_sb[:, b], ACT.Copy).then_inc(xhi_done, 1)

            def out0(b):
                act.wait_ge(apply_mm, 2 * b + 1)
                if b == 0:
                    act.wait_ge(bias_done, 1)
                if b >= 2:
                    act.wait_ge(stored[b % 2][0], 16 * (b // 2))
                nc.scalar.activation(out_sb[:, b % 2, 0, :], ps_out[b % 2][0][:, :], ACT.Identity,
                                     bias=bias_sb[:, 0, b:b + 1]).then_inc(out0_done, 1)

            a_hi(0)
            a_hi(1)
            for b in range(NB):
                w1_hi(b)
                if b + 2 < NB:
                    a_hi(b + 2)
            w0_hi(0)
            w0_hi(1)
            x_hi_(0)
            x_hi_(1)
            for b in range(NB):
                m_hi(b)
                if b + 2 < NB:
                    w0_hi(b + 2)
                if b >= 1:
                    out0(b - 1)
                    if b + 1 < NB:
                        x_hi_(b + 1)
            out0(NB - 1)

        @block.vector
        def _(dve):
            dve.wait_ge(small_in, 16)
            nc.vector.tensor_scalar(gate2[:, :], cond_er, SCALING, None, ALU.mult).then_inc(gate_done, 1)
            for j in range(NT):
                last = nc.vector.tensor_copy(bias0_rep[:, j, :], bias0[:, j:j + 1].to_broadcast([P, NB]))
            last.then_inc(rep_done, 1)
            dve.wait_ge(gate_done, 1)

            def a_lo(b):
                dve.wait_ge(ahi_done, b + 1)
                if b >= 2:
                    dve.wait_ge(lora_mm, b - 1)
                nc.vector.scalar_tensor_tensor(out=A_lo[:, b % 2], in0=A_er, scalar=gate2[:, b:b + 1],
                                               in1=A_hi[:, b % 2].bitcast(f32),
                                               op0=ALU.mult, op1=ALU.subtract).then_inc(alo_done, 1)

            def w1(b):
                dve.wait_ge(lora_mm, b + 1)
                nc.vector.tensor_tensor(W1[:, b], ps_lora[b % 2][:, :, :], base_sb[:, :, :],
                                        ALU.add).then_inc(w1_done, 1)

            def w0(s):
                j, i = s % NT, s // NT
                dve.wait_ge(mix_mm, s + 1)
                if s == 0:
                    dve.wait_ge(mask_in, 16)
                m = mask_sb[:, j, i * KPD * TB:(i + 1) * KPD * TB].rearrange("p (k t) -> p k t", t=TB)
                nc.vector.tensor_tensor(
                    W0[:, :, j, i * KPD * TB:(i + 1) * KPD * TB].rearrange("p b (k t) -> p k b t", t=TB),
                    ps_mix[s % 2][:, :].rearrange("p (k b t) -> p k b t", k=KPD, t=TB),
                    m.unsqueeze(2).to_broadcast([P, KPD, NB, TB]),
                    ALU.mult).then_inc(w0_done, 1)

            def x_lo_(b):
                dve.wait_ge(xhi_done, b + 1)
                if b >= 2:
                    dve.wait_ge(apply_mm, 2 * (b - 1))
                nc.vector.tensor_tensor(x_lo[:, b % 2], x_sb[:, b], x_hi[:, b % 2].bitcast(f32),
                                        ALU.subtract).then_inc(xlo_done, 1)

            def m(b):
                dve.wait_ge(merge_mm, b + 1)
                if b >= 2:
                    dve.wait_ge(mlo_done, b - 1)
                nc.vector.tensor_tensor(M[:, b % 2], ps_merge[b % 2][:, :, :], W1[:, b],
                                        ALU.add).then_inc(m_done, 1)

            def out1(b):
                dve.wait_ge(apply_mm, 2 * b + 2)
                if b >= 2:
                    dve.wait_ge(stored[b % 2][1], 16 * (b // 2))
                nc.vector.tensor_scalar(out_sb[:, b % 2, 1, :], ps_out[b % 2][1][:, :],
                                        bias_sb[:, 1, b:b + 1], None, ALU.add).then_inc(out1_done, 1)

            a_lo(0)
            dve.wait_ge(base_in, 16)
            dve.wait_ge(ident_done, 1)
            for j in range(NT):
                diag = base_sb[:, j, j * P:(j + 1) * P]
                last = nc.vector.tensor_tensor(diag, diag, ident[:, :], ALU.add)
            last.then_inc(base_done, 1)
            a_lo(1)
            dve.wait_ge(base_done, 1)
            dve.wait_ge(u_done, 1)
            nc.vector.tensor_scalar(low_bias[:, :], gate2[:, :], ps_bias[:, 0:1], None, ALU.mult).then_inc(low_done, 1)
            for b in range(NB):
                w1(b)
                if b + 2 < NB:
                    a_lo(b + 2)
                if b == 1:
                    dve.wait_ge(bias_mm, 1)
                    for j in range(NT):
                        last = nc.vector.tensor_scalar(bias_sb[:, j, :], ps_bias[:, 64 + j * NB:64 + (j + 1) * NB],
                                                       bias1[:, j:j + 1], None, ALU.add)
                    last.then_inc(bias_done, 1)
                if b == 3:
                    w0(0)
                    w0(1)
                if b >= 4:
                    for s in range(2 * (b - 3), min(2 * (b - 2), SLOTS)):
                        w0(s)
            x_lo_(0)
            x_lo_(1)
            for b in range(NB):
                m(b)
                if b >= 1:
                    out1(b - 1)
                    if b + 1 < NB:
                        x_lo_(b + 1)
            dve.wait_ge(bias_done, 1)
            out1(NB - 1)

        @block.tensor
        def _(pe):
            def three(out, hi_l, lo_l, hi_r, lo_r, first, last):
                nc.tensor.matmul(out, lo_l, hi_r, start=first, stop=False)
                nc.tensor.matmul(out, hi_l, lo_r, start=False, stop=False)
                return nc.tensor.matmul(out, hi_l, hi_r, start=False, stop=last)

            def lora(b):
                pe.wait_ge(alo_done, b + 1)
                if b == 0:
                    pe.wait_ge(blo_done, 1)
                if b >= 2:
                    pe.wait_ge(w1_done, b - 1)
                for j in range(NT):
                    cols = slice(j * P, (j + 1) * P)
                    mm = three(ps_lora[b % 2][:, j, :], A_hi[:, b % 2, cols], A_lo[:, b % 2, cols],
                               B_hi[:, :], B_lo[:, :], True, True)
                mm.then_inc(lora_mm, 1)

            def mixed(s):
                j, i = s % NT, s // NT
                pe.wait_ge(experts_in[i], 16)
                if s == 0:
                    pe.wait_ge(mix_in, 16)
                if s >= 2:
                    pe.wait_ge(w0_done, s - 1)
                for k in range(KPD):
                    mm = nc.tensor.matmul(ps_mix[s % 2][:, k * P:(k + 1) * P],
                                          experts_sb[:, i * KPD + k, j * P:(j + 1) * P], mix_sb[:, :],
                                          start=True, stop=True)
                mm.then_inc(mix_mm, 1)

            def merge(b):
                pe.wait_ge(w0lo_done, b + 1)
                pe.wait_ge(w1lo_done, b + 1)
                if b >= 2:
                    pe.wait_ge(m_done, b - 1)
                for i in range(NT):
                    for j in range(NT):
                        rows = slice(i * P, (i + 1) * P)
                        mm = three(ps_merge[b % 2][:, i, :], W0_hi[:, b % 2, j, rows], W0_lo[:, b % 2, j, rows],
                                   W1_hi[:, b, j], W1_lo[:, b, j], j == 0, j == NT - 1)
                mm.then_inc(merge_mm, 1)

            def apply(b):
                pe.wait_ge(mlo_done, b + 1)
                pe.wait_ge(xlo_done, b + 1)
                for i, done in enumerate((out0_done, out1_done)):
                    if b >= 2:
                        pe.wait_ge(done, b - 1)
                    cols = slice(i * P, (i + 1) * P)
                    for j in range(NT):
                        mm = three(ps_out[b % 2][i][:, :], M_hi[:, b % 2, j, cols], M_lo[:, b % 2, j, cols],
                                   x_hi[:, b % 2, j], x_lo[:, b % 2, j], j == 0, j == NT - 1)
                    mm.then_inc(apply_mm, 1)

            pe.wait_ge(small_in, 16)
            for j in range(NT):
                mm = nc.tensor.matmul(ps_bias[:, 0:1], A_t[:, j, :], bias0[:, j:j + 1], start=(j == 0), stop=(j == NT - 1))
            mm.then_inc(u_done, 1)
            lora(0)
            lora(1)
            pe.wait_ge(low_done, 1)
            pe.wait_ge(rep_done, 1)
            pe.wait_ge(base_done, 1)
            for i in range(NT):
                cols = slice(i * P, (i + 1) * P)
                dst = ps_bias[:, 64 + i * NB:64 + (i + 1) * NB]
                for j in range(NT):
                    nc.tensor.matmul(dst, base_sb[:, j, cols], bias0_rep[:, j, :], start=(j == 0), stop=False)
                mm = nc.tensor.matmul(dst, B_er[:, cols], low_bias[:, :], start=False, stop=True)
            mm.then_inc(bias_mm, 1)
            lora(2)
            lora(3)
            mixed(0)
            mixed(1)
            for b in range(4, NB):
                lora(b)
                for s in range(2 * (b - 3), min(2 * (b - 2), SLOTS)):
                    mixed(s)
            merge(0)
            pe.wait_ge(w0_done, SLOTS)
            pe.wait_ge(bias_done, 1)
            for b in range(NB):
                if b + 1 < NB:
                    merge(b + 1)
                apply(b)


def kernel(x, cond_8, L0_cond_weight, L0_cond_mask, L0_cond_bias,
           L1_cond_W_base, L1_cond_b_base, L1_cond_As, L1_cond_Bs):
    import numpy as np
    import concourse.bacc as bacc
    from concourse.bass_utils import run_bass_kernel_spmd

    P = 128
    x, cond, weight, mask, bias0, base, bias1, As, Bs = (
        np.asarray(a) for a in (x, cond_8, L0_cond_weight, L0_cond_mask, L0_cond_bias,
                                L1_cond_W_base, L1_cond_b_base, L1_cond_As, L1_cond_Bs))
    NB, TOK, C = x.shape
    G = weight.shape[0]
    NT = C // P
    TB = P // G
    R = As.shape[1]

    def halves(a):
        return np.ascontiguousarray(a.reshape(NT, P, -1).transpose(1, 0, 2).reshape(P, -1))

    experts = np.ascontiguousarray(weight.reshape(G, C, C // TB, TB).transpose(0, 3, 2, 1).reshape(P, C // TB, C))
    mix = np.zeros((G, TB, NB, TB), cond.dtype)
    for t in range(TB):
        mix[:, t, :, t] = cond.T
    A_er = As.reshape(G * R, C)
    small = np.concatenate([np.repeat(cond.T, R, axis=0), halves(bias0[:, None]), halves(bias1[:, None]),
                            halves(A_er.T), A_er, Bs.transpose(0, 2, 1).reshape(G * R, C)], axis=1)
    xT = np.ascontiguousarray(x.transpose(0, 2, 1).reshape(NB, NT, P, TOK).transpose(0, 2, 1, 3).reshape(NB, P, NT * TOK))
    arrays = {"experts": experts, "small": np.ascontiguousarray(small), "mix": mix.reshape(P, P),
              "base": halves(base.T), "mask": halves(mask), "xT": xT}

    nc = bacc.Bacc("TRN2", target_bir_lowering=False, num_devices=1)
    f32 = mybir.dt.float32
    args = [nc.dram_tensor(f"{n}_dram", a.shape, f32, kind="ExternalInput").ap() for n, a in arrays.items()]
    outT = nc.dram_tensor("outT_dram", (NB, NT, P, TOK), f32, kind="ExternalOutput").ap()
    conditional_residual_kernel(nc, *args, outT)
    r = run_bass_kernel_spmd(nc, [{f"{n}_dram": a for n, a in arrays.items()}], core_ids=[0])
    got = np.asarray(r.results[0]["outT_dram"])
    return np.ascontiguousarray(got.reshape(NB, C, TOK).transpose(0, 2, 1))
```

```python
import concourse.bass as bass
from concourse import mybir
from contextlib import ExitStack


def conditional_residual_kernel(nc: bass.Bass, packs: bass.AP, lora_in: bass.AP, base: bass.AP,
                                first_lora: bass.AP, xT: bass.AP, outT: bass.AP):
    f32 = mybir.dt.float32
    f32r = mybir.dt.float32r
    bf16 = mybir.dt.bfloat16
    ALU = mybir.AluOpType
    ACT = mybir.ActivationFunctionType

    P = 128
    NB, _, XW = xT.shape
    NT = 2
    TOK = XW // NT
    C = base.shape[1] // NT
    H = P
    NG = 8
    TB = P // NG
    KQ = 2
    TQ = KQ * TB
    NQ = C // TQ
    MIXW = P
    EXPW = KQ * C
    PACKW = EXPW + NT * TQ
    SCALING = 32.0 / 16
    LEAD = 4
    XBUF = 4
    W1BUF = 4
    WARM = 10
    assert packs.shape[1] == MIXW + NQ * PACKW
    OB0, OB1, OA, OBT = NB, NB + NT, NB + 2 * NT, NB + 2 * NT + C

    with ExitStack() as ctx:
        def sb(name, shape, dt=f32):
            return ctx.enter_context(nc.sbuf_tensor(name, shape, dt))

        def pb(name, shape):
            return ctx.enter_context(nc.psum_tensor(name, shape, f32))

        def sem(name):
            return ctx.enter_context(nc.semaphore(name))

        packs_sb = sb("packs_sb", [P, MIXW + NQ * PACKW])
        mix = packs_sb[:, 0:MIXW]

        def pack(q):
            at = MIXW + q * PACKW
            return (packs_sb[:, at:at + EXPW].rearrange("p (k c) -> p k c", k=KQ),
                    packs_sb[:, at + EXPW:at + PACKW].rearrange("p (j t) -> p j t", j=NT))

        lora_sb = sb("lora_sb", [P, OBT + C])
        cond_er = lora_sb[:, 0:NB]
        bias0 = lora_sb[:, OB0:OB0 + NT]
        bias1 = lora_sb[:, OB1:OB1 + NT]
        A_er = lora_sb[:, OA:OA + C]
        B_er = lora_sb[:, OBT:OBT + C]
        base_sb = sb("base_sb", [P, NT, C])
        A_t = sb("A_t", [P, NT, P])
        x_sb = sb("x_sb", [P, NB, NT, TOK])
        warm = sb("warm", [P, 512], bf16)
        ident = sb("ident", [P, P])
        bias0_rep = sb("bias0_rep", [P, NT, NB])
        low_bias = sb("low_bias", [P, NB])
        bias_sb = sb("bias_sb", [P, NT, NB])
        B_hi = sb("B_hi", [P, C], f32r)
        B_lo = sb("B_lo", [P, C], f32r)
        A_hi = sb("A_hi", [P, 2, C], f32r)
        A_lo = sb("A_lo", [P, 2, C], f32r)
        W1 = sb("W1", [P, W1BUF, NT, C])
        W1_hi = sb("W1_hi", [P, W1BUF, NT, C], f32r)
        W1_lo = sb("W1_lo", [P, W1BUF, NT, C], f32r)
        W0 = sb("W0", [P, NB, NT, C])
        W0_hi = sb("W0_hi", [P, 2, NT, C], f32r)
        W0_lo = sb("W0_lo", [P, 2, NT, C], f32r)
        M = sb("M", [P, 2, NT, C])
        M_hi = sb("M_hi", [P, 2, NT, C], f32r)
        M_lo = sb("M_lo", [P, 2, NT, C], f32r)
        x_hi = sb("x_hi", [P, XBUF, NT, TOK], f32r)
        x_lo = sb("x_lo", [P, XBUF, NT, TOK], f32r)
        out_sb = sb("out_sb", [P, 2, NT, TOK])

        ps_out = [pb(f"ps_out{i}", [P, TOK]) for i in range(2 * NT)]
        ps_merge = [pb(f"ps_merge{i}", [P, NT, C]) for i in range(2)]
        ps_lora = [pb(f"ps_lora{i}", [P, NT, C]) for i in range(2)]
        ps_mix = ps_out
        ps_last = ps_lora[0][:, 0, :]
        ps_low = ps_out[3][:, 0:1]
        ps_bias = ps_out[3][:, 64:64 + NT * NB].rearrange("p (j b) -> p j b", j=NT)

        mix_in, lora_arrived, base_in, first_lora_in = sem("mix_in"), sem("lora_arrived"), sem("base_in"), sem("first_lora_in")
        pack_in = [sem(f"pack_in{q}") for q in range(NQ)]
        x_in = [sem(f"x_in{b}") for b in range(NB)]
        warm_set, ident_zero, ident_done = sem("warm_set"), sem("ident_zero"), sem("ident_done")
        base_done, rep_done, low_mm, low_done = sem("base_done"), sem("rep_done"), sem("low_mm"), sem("low_done")
        bias_mm, bias_done, bhi_done, blo_done = sem("bias_mm"), sem("bias_done"), sem("bhi_done"), sem("blo_done")
        ahi_done, alo_done = sem("ahi_done"), sem("alo_done")
        lora_mm, w1_done, w1hi_done, w1lo_done = sem("lora_mm"), sem("w1_done"), sem("w1hi_done"), sem("w1lo_done")
        mix_mm, w0_done, w0hi_done, w0lo_done = sem("mix_mm"), sem("w0_done"), sem("w0hi_done"), sem("w0lo_done")
        w0hi_first, w0lo_first, w0lo_second = sem("w0hi_first"), sem("w0lo_first"), sem("w0lo_second")
        mlo_first = sem("mlo_first")
        merge_mm, m_done, mhi_done, mlo_done = sem("merge_mm"), sem("m_done"), sem("mhi_done"), sem("mlo_done")
        xhi_done, xlo_done = sem("xhi_done"), sem("xlo_done")
        apply_mm = sem("apply_mm")
        out_done = [sem(f"out_done{j}") for j in range(NT)]
        last_done = sem("last_done")
        stored = [[sem(f"stored{i}{j}") for j in range(NT)] for i in range(2)]

        block = ctx.enter_context(nc.Block())

        @block.sync
        def _(sp):
            def load_pack(q):
                at = MIXW + q * PACKW
                sp.dma_start(packs_sb[:, at:at + PACKW], packs[:, at:at + PACKW]).then_inc(pack_in[q], 16)

            head = MIXW + C
            sp.dma_start(packs_sb[:, 0:head], packs[:, 0:head]).then_inc(mix_in, 16)
            sp.dma_start(packs_sb[:, head:MIXW + PACKW], packs[:, head:MIXW + PACKW]).then_inc(pack_in[0], 16)
            sp.dma_start(lora_sb[:, :], lora_in).then_inc(lora_arrived, 16)
            load_pack(1)
            load_pack(2)
            sp.dma_start(base_sb[:, :, :], base.rearrange("p (j o) -> p j o", j=NT)).then_inc(base_in, 16)
            for q in range(3, NQ):
                load_pack(q)
            for b in range(NB):
                sp.dma_start(x_sb[:, b], xT[b].rearrange("p (j n) -> p j n", j=NT)).then_inc(x_in[b], 16)
                if b == 0:
                    sp.dma_start(A_t[:, :, :], first_lora.rearrange("p (j e) -> p j e", j=NT)).then_inc(first_lora_in, 16)
            for b in range(NB):
                for j in range(NT):
                    if b < NB - 1 or j < NT - 1:
                        sp.wait_ge(out_done[j], b + 1)
                        sp.dma_start(outT[b, j], out_sb[:, b % 2, j, :]).then_inc(stored[b % 2][j], 16)
            sp.wait_ge(last_done, 1)
            sp.dma_start(outT[NB - 1, 1, :, 0:TOK // 2],
                         out_sb[:, 1, 1, 0:TOK // 2]).then_inc(stored[1][1], 16)
            sp.wait_ge(out_done[1], NB)
            sp.dma_start(outT[NB - 1, 1, :, TOK // 2:TOK],
                         out_sb[:, 1, 1, TOK // 2:TOK]).then_inc(stored[1][1], 16)
            for i in range(2):
                for j in range(NT):
                    sp.wait_ge(stored[i][j], 16 * (NB // 2 + (i == 1 and j == 1)))

        @block.gpsimd
        def _(pool):
            pool.memset(ident[:, :], 0.0).then_inc(ident_zero, 1)
            pool.wait_ge(ident_zero, 1)
            pool.affine_select(out=ident[:, :], in_=ident[:, :], compare_op=ALU.not_equal, fill=1.0,
                               base=0, pattern=[[-1, P]], channel_multiplier=1).then_inc(ident_done, 1)

            def w1_lo(b):
                pool.wait_ge(w1hi_done, b + 1)
                if b >= W1BUF:
                    pool.wait_ge(merge_mm, b - W1BUF + 1)
                pool.tensor_tensor(W1_lo[:, b % W1BUF], W1[:, b % W1BUF], W1_hi[:, b % W1BUF].bitcast(f32),
                                   ALU.subtract).then_inc(w1lo_done, 1)

            def w0_lo(b):
                pool.wait_ge(w0hi_done, b + 1)
                if b >= 2:
                    pool.wait_ge(merge_mm, b - 1)
                pool.tensor_tensor(W0_lo[:, b % 2], W0[:, b], W0_hi[:, b % 2].bitcast(f32),
                                   ALU.subtract).then_inc(w0lo_done, 1)

            def m_lo(b):
                pool.wait_ge(mhi_done, b + 1)
                if b >= 2:
                    pool.wait_ge(apply_mm, 2 * (b - 1))
                pool.tensor_tensor(M_lo[:, b % 2], M[:, b % 2], M_hi[:, b % 2].bitcast(f32),
                                   ALU.subtract).then_inc(mlo_done, 1)

            w1_lo(0)
            pool.wait_ge(w0hi_first, 1)
            pool.tensor_tensor(W0_lo[:, 0, :, 0:H], W0[:, 0, :, 0:H], W0_hi[:, 0, :, 0:H].bitcast(f32),
                               ALU.subtract).then_inc(w0lo_first, 1)
            w1_lo(1)
            w0_lo(1)
            w1_lo(2)
            w1_lo(3)
            for b in range(NB):
                if 2 <= b + 2 < NB:
                    w0_lo(b + 2)
                if 4 <= b + 3 < NB:
                    w1_lo(b + 3)
                if b + 1 < NB:
                    m_lo(b + 1)

        @block.scalar
        def _(act):
            def a_hi(b):
                if b >= 2:
                    act.wait_ge(lora_mm, b - 1)
                nc.scalar.activation(A_hi[:, b % 2], A_er, ACT.Copy,
                                     scale=cond_er[:, b:b + 1]).then_inc(ahi_done, 1)

            def w1_hi(b):
                act.wait_ge(w1_done, b + 1)
                if b >= W1BUF:
                    act.wait_ge(merge_mm, b - W1BUF + 1)
                nc.scalar.activation(W1_hi[:, b % W1BUF], W1[:, b % W1BUF], ACT.Copy).then_inc(w1hi_done, 1)

            def w0_hi(b):
                if b >= 2:
                    act.wait_ge(merge_mm, b - 1)
                nc.scalar.activation(W0_hi[:, b % 2], W0[:, b], ACT.Copy).then_inc(w0hi_done, 1)

            def m_hi(b):
                act.wait_ge(m_done, b + 1)
                if b >= 2:
                    act.wait_ge(apply_mm, 2 * (b - 1))
                nc.scalar.activation(M_hi[:, b % 2], M[:, b % 2], ACT.Copy).then_inc(mhi_done, 1)

            def split_x_hi(b):
                act.wait_ge(x_in[b], 16)
                if b >= XBUF:
                    act.wait_ge(apply_mm, 2 * (b - XBUF + 1))
                nc.scalar.activation(x_hi[:, b % XBUF], x_sb[:, b], ACT.Copy).then_inc(xhi_done, 1)

            def out0(b):
                act.wait_ge(apply_mm, 2 * b + 1)
                if b == 0:
                    act.wait_ge(bias_done, 1)
                if b >= 2:
                    act.wait_ge(stored[b % 2][0], 16 * (b // 2))
                nc.scalar.activation(out_sb[:, b % 2, 0, :], ps_out[b % 2 * NT][:, :], ACT.Identity,
                                     bias=bias_sb[:, 0, b:b + 1]).then_inc(out_done[0], 1)

            act.wait_ge(lora_arrived, 16)
            a_hi(0)
            nc.scalar.activation(B_hi[:, :], B_er, ACT.Copy, scale=SCALING).then_inc(bhi_done, 1)
            a_hi(1)
            w1_hi(0)
            a_hi(2)
            act.wait_ge(w0_done, NQ // 2)
            nc.scalar.activation(W0_hi[:, 0, :, 0:H], W0[:, 0, :, 0:H], ACT.Copy).then_inc(w0hi_first, 1)
            w1_hi(1)
            a_hi(3)
            w1_hi(2)
            split_x_hi(0)
            act.wait_ge(w0_done, NQ)
            nc.scalar.activation(W0_hi[:, 0, :, H:C], W0[:, 0, :, H:C], ACT.Copy).then_inc(w0hi_done, 1)
            w0_hi(1)
            w1_hi(3)
            m_hi(0)
            split_x_hi(1)
            w0_hi(2)
            split_x_hi(2)
            for b in range(NB):
                if 4 <= b + 3 < NB:
                    w1_hi(b + 3)
                if b + 4 < NB:
                    a_hi(b + 4)
                if b + 1 < NB:
                    m_hi(b + 1)
                if b + 3 < NB:
                    split_x_hi(b + 3)
                out0(b)
                if b + 3 < NB:
                    w0_hi(b + 3)
            b = NB - 1
            act.wait_ge(apply_mm, 2 * b + 2)
            act.wait_ge(stored[b % 2][1], 16 * (b // 2))
            nc.scalar.activation(out_sb[:, b % 2, 1, 0:TOK // 2], ps_out[b % 2 * NT + 1][:, 0:TOK // 2], ACT.Identity,
                                 bias=bias_sb[:, 1, b:b + 1]).then_inc(last_done, 1)

        @block.vector
        def _(dve):
            nc.vector.memset(warm[:, :], 0.0).then_inc(warm_set, 1)

            def a_lo(b):
                dve.wait_ge(ahi_done, b + 1)
                if b >= 2:
                    dve.wait_ge(lora_mm, b - 1)
                nc.vector.scalar_tensor_tensor(out=A_lo[:, b % 2], in0=A_er, scalar=cond_er[:, b:b + 1],
                                               in1=A_hi[:, b % 2].bitcast(f32),
                                               op0=ALU.mult, op1=ALU.subtract).then_inc(alo_done, 1)

            def w1(b):
                dve.wait_ge(lora_mm, b + 1)
                if b >= W1BUF:
                    dve.wait_ge(m_done, b - W1BUF + 1)
                    dve.wait_ge(w1lo_done, b - W1BUF + 1)
                nc.vector.tensor_tensor(W1[:, b % W1BUF], ps_lora[b % 2][:, :, :], base_sb[:, :, :],
                                        ALU.add).then_inc(w1_done, 1)

            def w0(q):
                dve.wait_ge(mix_mm, q + 1)
                dve.wait_ge(pack_in[q], 16)
                ts = slice(q * TQ, (q + 1) * TQ)
                nc.vector.tensor_tensor(
                    W0[:, :, :, ts].rearrange("p b j t -> p j b t"),
                    ps_mix[q % 4][:, :].rearrange("p (j b t) -> p j b t", j=NT, t=TQ),
                    pack(q)[1].unsqueeze(2).to_broadcast([P, NT, NB, TQ]),
                    ALU.mult).then_inc(w0_done, 1)

            def split_x_lo(b):
                dve.wait_ge(xhi_done, b + 1)
                if b >= XBUF:
                    dve.wait_ge(apply_mm, 2 * (b - XBUF + 1))
                nc.vector.tensor_tensor(x_lo[:, b % XBUF], x_sb[:, b], x_hi[:, b % XBUF].bitcast(f32),
                                        ALU.subtract).then_inc(xlo_done, 1)

            def m(b):
                dve.wait_ge(merge_mm, b + 1)
                if b == 2:
                    dve.wait_ge(mlo_first, 1)
                if b >= 3:
                    dve.wait_ge(mlo_done, b - 2)
                nc.vector.tensor_tensor(M[:, b % 2], ps_merge[b % 2][:, :, :], W1[:, b % W1BUF],
                                        ALU.add).then_inc(m_done, 1)

            def out1(b):
                dve.wait_ge(apply_mm, 2 * b + 2)
                if b >= 2:
                    dve.wait_ge(stored[b % 2][1], 16 * (b // 2))
                nc.vector.tensor_scalar(out_sb[:, b % 2, 1, :], ps_out[b % 2 * NT + 1][:, :],
                                        bias_sb[:, 1, b:b + 1], None, ALU.add).then_inc(out_done[1], 1)

            w0(0)
            a_lo(0)
            dve.wait_ge(bhi_done, 1)
            nc.vector.scalar_tensor_tensor(out=B_lo[:, :], in0=B_er, scalar=SCALING, in1=B_hi[:, :].bitcast(f32),
                                           op0=ALU.mult, op1=ALU.subtract).then_inc(blo_done, 1)
            a_lo(1)
            w0(1)
            dve.wait_ge(base_in, 16)
            dve.wait_ge(ident_done, 1)
            for j in range(NT):
                diag = base_sb[:, j, j * P:(j + 1) * P]
                last = nc.vector.tensor_tensor(diag, diag, ident[:, :], ALU.add)
            last.then_inc(base_done, 1)
            dve.wait_ge(base_done, 1)
            w1(0)
            w0(2)
            w0(3)
            a_lo(2)
            w1(1)
            w0(4)
            w0(5)
            a_lo(3)
            w1(2)
            w0(6)
            w0(7)
            dve.wait_ge(w0hi_done, 1)
            nc.vector.tensor_tensor(W0_lo[:, 0, :, H:C], W0[:, 0, :, H:C], W0_hi[:, 0, :, H:C].bitcast(f32),
                                    ALU.subtract).then_inc(w0lo_second, 1)
            w1(3)
            for j in range(NT):
                last = nc.vector.tensor_copy(bias0_rep[:, j, :], bias0[:, j:j + 1].to_broadcast([P, NB]))
            last.then_inc(rep_done, 1)
            dve.wait_ge(low_mm, 1)
            nc.vector.tensor_scalar(low_bias[:, :], cond_er, ps_low, SCALING, ALU.mult, ALU.mult).then_inc(low_done, 1)
            split_x_lo(0)
            m(0)
            dve.wait_ge(mhi_done, 1)
            nc.vector.tensor_tensor(M_lo[:, 0], M[:, 0], M_hi[:, 0].bitcast(f32), ALU.subtract).then_inc(mlo_first, 1)
            dve.wait_ge(bias_mm, 1)
            for j in range(NT):
                last = nc.vector.tensor_scalar(bias_sb[:, j, :], ps_bias[:, j, :], bias1[:, j:j + 1], None, ALU.add)
            last.then_inc(bias_done, 1)
            dve.wait_ge(bias_done, 1)
            for b in range(NB):
                if 4 <= b + 3 < NB:
                    w1(b + 3)
                if b >= 1:
                    out1(b - 1)
                if b + 1 < NB:
                    m(b + 1)
                if b + 4 < NB:
                    a_lo(b + 4)
                if b == 0:
                    split_x_lo(1)
                if b + 2 < NB:
                    split_x_lo(b + 2)
            b = NB - 1
            dve.wait_ge(apply_mm, 2 * b + 3)
            dve.wait_ge(stored[b % 2][1], 16 * (b // 2))
            nc.vector.tensor_scalar(out_sb[:, b % 2, 1, TOK // 2:TOK], ps_last,
                                    bias_sb[:, 1, b:b + 1], None, ALU.add).then_inc(out_done[1], 1)

        @block.tensor
        def _(pe):
            def three(out, hi_l, lo_l, hi_r, lo_r, first, last):
                nc.tensor.matmul(out, hi_l, hi_r, start=first, stop=False)
                nc.tensor.matmul(out, lo_l, hi_r, start=False, stop=False)
                return nc.tensor.matmul(out, hi_l, lo_r, start=False, stop=last)

            def lora(b):
                pe.wait_ge(alo_done, b + 1)
                if b == 0:
                    pe.wait_ge(blo_done, 1)
                if b >= 2:
                    pe.wait_ge(w1_done, b - 1)
                for j in range(NT):
                    cols = slice(j * P, (j + 1) * P)
                    mm = three(ps_lora[b % 2][:, j, :], A_hi[:, b % 2, cols], A_lo[:, b % 2, cols],
                               B_hi[:, :], B_lo[:, :], True, True)
                mm.then_inc(lora_mm, 1)

            def mixed(q):
                if q == 0:
                    pe.wait_ge(mix_in, 16)
                else:
                    pe.wait_ge(pack_in[q], 16)
                if q >= 4:
                    pe.wait_ge(w0_done, q - 3)
                dst = ps_mix[q % 4][:, :].rearrange("p (j b k t) -> p j b k t", j=NT, k=KQ, t=TB)
                for k in range(KQ):
                    if q == 0 and k == 1:
                        pe.wait_ge(pack_in[0], 16)
                    for j in range(NT):
                        mm = nc.tensor.matmul(dst[:, j, :, k, :], pack(q)[0][:, k, j * P:(j + 1) * P], mix,
                                              start=True, stop=True)
                mm.then_inc(mix_mm, 1)

            def merge_half(b, i):
                rows = slice(i * P, (i + 1) * P)
                for j in range(NT):
                    mm = three(ps_merge[b % 2][:, i, :], W0_hi[:, b % 2, j, rows], W0_lo[:, b % 2, j, rows],
                               W1_hi[:, b % W1BUF, j], W1_lo[:, b % W1BUF, j], j == 0, j == NT - 1)
                return mm

            def merge(b):
                pe.wait_ge(w0lo_done, b)
                pe.wait_ge(w1lo_done, b + 1)
                if b >= 2:
                    pe.wait_ge(m_done, b - 1)
                merge_half(b, 0)
                merge_half(b, 1).then_inc(merge_mm, 1)

            def apply(b):
                if b == 0:
                    pe.wait_ge(mlo_first, 1)
                else:
                    pe.wait_ge(mlo_done, b)
                pe.wait_ge(xlo_done, b + 1)
                for i in range(NT):
                    if b >= 2:
                        pe.wait_ge(out_done[i], b - 1)
                    cols = slice(i * P, (i + 1) * P)
                    whole = b < NB - 1 or i < NT - 1
                    for n in [slice(0, TOK)] if whole else [slice(0, TOK // 2), slice(TOK // 2, TOK)]:
                        for j in range(NT):
                            bank = ps_out[b % 2 * NT + i][:, n] if n.start == 0 else ps_last
                            mm = three(bank, M_hi[:, b % 2, j, cols], M_lo[:, b % 2, j, cols],
                                       x_hi[:, b % XBUF, j, n], x_lo[:, b % XBUF, j, n], j == 0, j == NT - 1)
                        mm.then_inc(apply_mm, 1)

            pe.wait_ge(warm_set, 1)
            for _ in range(WARM):
                nc.tensor.matmul(ps_merge[0][:, :, :], warm[:, 0:P], warm[:, :], start=True, stop=True)
            mixed(0)
            lora(0)
            mixed(1)
            lora(1)
            mixed(2)
            mixed(3)
            mixed(4)
            lora(2)
            mixed(5)
            mixed(6)
            mixed(7)
            pe.wait_ge(w0lo_first, 1)
            pe.wait_ge(w1lo_done, 1)
            merge_half(0, 0)
            lora(3)
            pe.wait_ge(w0lo_second, 1)
            merge_half(0, 1).then_inc(merge_mm, 1)
            pe.wait_ge(first_lora_in, 16)
            pe.wait_ge(w0_done, NQ)
            for j in range(NT):
                mm = nc.tensor.matmul(ps_low, A_t[:, j, :], bias0[:, j:j + 1], start=(j == 0), stop=(j == NT - 1))
            mm.then_inc(low_mm, 1)
            merge(1)
            pe.wait_ge(low_done, 1)
            pe.wait_ge(rep_done, 1)
            pe.wait_ge(base_done, 1)
            for i in range(NT):
                cols = slice(i * P, (i + 1) * P)
                for j in range(NT):
                    nc.tensor.matmul(ps_bias[:, i, :], base_sb[:, j, cols], bias0_rep[:, j, :], start=(j == 0), stop=False)
                mm = nc.tensor.matmul(ps_bias[:, i, :], B_er[:, cols], low_bias[:, :], start=False, stop=True)
            mm.then_inc(bias_mm, 1)
            apply(0)
            lora(4)
            pe.wait_ge(bias_done, 1)
            for b in range(1, NB):
                if b + 1 < NB:
                    merge(b + 1)
                apply(b)
                if b + LEAD < NB:
                    lora(b + LEAD)


def kernel(x, cond_8, L0_cond_weight, L0_cond_mask, L0_cond_bias,
           L1_cond_W_base, L1_cond_b_base, L1_cond_As, L1_cond_Bs):
    import numpy as np
    import concourse.bacc as bacc
    from concourse.bass_utils import run_bass_kernel_spmd

    P = 128
    x, cond, weight, mask, bias0, base, bias1, As, Bs = (
        np.asarray(a) for a in (x, cond_8, L0_cond_weight, L0_cond_mask, L0_cond_bias,
                                L1_cond_W_base, L1_cond_b_base, L1_cond_As, L1_cond_Bs))
    NB, TOK, C = x.shape
    G = weight.shape[0]
    NT = C // P
    TB = P // G
    R = As.shape[1]

    def halves(a):
        return np.ascontiguousarray(a.reshape(NT, P, -1).transpose(1, 0, 2).reshape(P, -1))

    KQ = 2
    TQ = KQ * TB
    NQ = C // TQ
    mix = np.zeros((G, TB, NB, TB), cond.dtype)
    for t in range(TB):
        mix[:, t, :, t] = cond.T
    experts = weight.reshape(G, C, NQ, KQ, TB).transpose(0, 4, 2, 3, 1).reshape(P, NQ, KQ * C)
    masks = mask.reshape(NT, P, NQ, TQ).transpose(1, 2, 0, 3).reshape(P, NQ, NT * TQ)
    packs = np.concatenate([mix.reshape(P, P), np.concatenate([experts, masks], axis=2).reshape(P, -1)], axis=1)
    A_er = As.reshape(G * R, C)
    lora = np.concatenate([np.repeat(cond.T, R, axis=0), halves(bias0[:, None]), halves(bias1[:, None]),
                           A_er, Bs.transpose(0, 2, 1).reshape(G * R, C)], axis=1)
    xT = np.ascontiguousarray(x.transpose(0, 2, 1).reshape(NB, NT, P, TOK).transpose(0, 2, 1, 3).reshape(NB, P, NT * TOK))
    arrays = {"packs": packs, "lora": lora, "base": halves(base.T), "first_lora": halves(A_er.T), "xT": xT}
    arrays = {n: np.ascontiguousarray(a) for n, a in arrays.items()}

    nc = bacc.Bacc("TRN2", target_bir_lowering=False, num_devices=1)
    f32 = mybir.dt.float32
    args = [nc.dram_tensor(f"{n}_dram", a.shape, f32, kind="ExternalInput").ap() for n, a in arrays.items()]
    outT = nc.dram_tensor("outT_dram", (NB, NT, P, TOK), f32, kind="ExternalOutput").ap()
    conditional_residual_kernel(nc, *args, outT)
    r = run_bass_kernel_spmd(nc, [{f"{n}_dram": a for n, a in arrays.items()}], core_ids=[0])
    got = np.asarray(r.results[0]["outT_dram"])
    return np.ascontiguousarray(got.reshape(NB, C, TOK).transpose(0, 2, 1))
```

```python
import concourse.bass as bass
from concourse import mybir
from contextlib import ExitStack


def conditional_residual_kernel(nc: bass.Bass, packs: bass.AP, lora_in: bass.AP, base: bass.AP,
                                rows: bass.AP, xT: bass.AP, outT: bass.AP):
    f32 = mybir.dt.float32
    f32r = mybir.dt.float32r
    bf16 = mybir.dt.bfloat16
    ALU = mybir.AluOpType
    ACT = mybir.ActivationFunctionType

    P = 128
    NB, _, XW = xT.shape
    NT = 2
    TOK = XW // NT
    C = base.shape[1] // NT
    H = P
    NG = 8
    TB = P // NG
    KQ = 2
    TQ = KQ * TB
    NQ = C // TQ
    MIXW = P
    EXPW = KQ * C
    PACKW = EXPW + NT * TQ
    SCALING = 32.0 / 16
    EARLY = 6
    LEAD = 4
    XBUF = 4
    W1BUF = 4
    WARM = 21
    assert packs.shape[1] == MIXW + NQ * PACKW
    OB0, OB1, OA, OBT = NB, NB + NT, NB + 2 * NT, NB + 2 * NT + C

    with ExitStack() as ctx:
        def sb(name, shape, dt=f32):
            return ctx.enter_context(nc.sbuf_tensor(name, shape, dt))

        def pb(name, shape):
            return ctx.enter_context(nc.psum_tensor(name, shape, f32))

        def sem(name):
            return ctx.enter_context(nc.semaphore(name))

        packs_sb = sb("packs_sb", [P, MIXW + NQ * PACKW])
        mix = packs_sb[:, 0:MIXW]

        def pack(q):
            at = MIXW + q * PACKW
            return (packs_sb[:, at:at + EXPW].rearrange("p (k c) -> p k c", k=KQ),
                    packs_sb[:, at + EXPW:at + PACKW].rearrange("p (j t) -> p j t", j=NT))

        lora_sb = sb("lora_sb", [P, OBT + C])
        cond_er = lora_sb[:, 0:NB]
        bias0 = lora_sb[:, OB0:OB0 + NT]
        bias1 = lora_sb[:, OB1:OB1 + NT]
        A_er = lora_sb[:, OA:OA + C]
        B_er = lora_sb[:, OBT:OBT + C]
        base_sb = sb("base_sb", [P, NT, C])
        rows_sb = sb("rows_sb", [P, NT + 1, C])
        base_rows = rows_sb[:, 0:NT, :]
        bias0_row = rows_sb[:, NT, :]
        x_sb = sb("x_sb", [P, NB, NT, TOK])
        warm = sb("warm", [P, 128], bf16)
        ident = sb("ident", [P, P])
        row_products = sb("row_products", [P, C])
        A_bias0 = sb("A_bias0", [P, 1])
        base_bias0 = sb("base_bias0", [P, NT])
        bias_sum = sb("bias_sum", [P, NT])
        fixed_bias = sb("fixed_bias", [P, NT])
        low_bias = sb("low_bias", [P, NB])
        bias_sb = sb("bias_sb", [P, NT, NB])
        B_hi = sb("B_hi", [P, C], f32r)
        B_lo = sb("B_lo", [P, C], f32r)
        A_hi = sb("A_hi", [P, NB, C], f32r)
        A_lo = sb("A_lo", [P, NB, C], f32r)
        W1 = sb("W1", [P, W1BUF, NT, C])
        W1_hi = sb("W1_hi", [P, W1BUF, NT, C], f32r)
        W1_lo = sb("W1_lo", [P, W1BUF, NT, C], f32r)
        W0 = sb("W0", [P, NB, NT, C])
        W0_hi = sb("W0_hi", [P, 2, NT, C], f32r)
        W0_lo = sb("W0_lo", [P, 2, NT, C], f32r)
        M = sb("M", [P, 2, NT, C])
        M_hi = sb("M_hi", [P, 2, NT, C], f32r)
        M_lo = sb("M_lo", [P, 2, NT, C], f32r)
        x_hi = sb("x_hi", [P, XBUF, NT, TOK], f32r)
        x_lo = sb("x_lo", [P, XBUF, NT, TOK], f32r)
        out_sb = sb("out_sb", [P, 2, NT, TOK])

        ps_out = [pb(f"ps_out{i}", [P, TOK]) for i in range(2 * NT)]
        ps_merge = [pb(f"ps_merge{i}", [P, NT, C]) for i in range(2)]
        ps_lora = [pb(f"ps_lora{i}", [P, NT, C]) for i in range(2)]
        ps_mix = ps_out
        ps_last = ps_lora[0][:, 0, :]
        ps_bias = ps_out[3][:, 0:NT * NB].rearrange("p (j b) -> p j b", j=NT)

        mix_in, lora_arrived, base_in, rows_in = sem("mix_in"), sem("lora_arrived"), sem("base_in"), sem("rows_in")
        pack_in = [sem(f"pack_in{q}") for q in range(NQ)]
        x_in = [sem(f"x_in{b}") for b in range(NB)]
        warm_set, ident_zero, ident_done = sem("warm_set"), sem("ident_zero"), sem("ident_done")
        base_done, dots_done, low_done, fixed_done = sem("base_done"), sem("dots_done"), sem("low_done"), sem("fixed_done")
        bias_mm, bias_done, bhi_done, blo_done = sem("bias_mm"), sem("bias_done"), sem("bhi_done"), sem("blo_done")
        ahi_done, alo_done = sem("ahi_done"), sem("alo_done")
        lora_mm, w1_done, w1hi_done, w1lo_done = sem("lora_mm"), sem("w1_done"), sem("w1hi_done"), sem("w1lo_done")
        mix_mm, w0_done, w0hi_done, w0lo_done = sem("mix_mm"), sem("w0_done"), sem("w0hi_done"), sem("w0lo_done")
        w0hi_first, w0lo_first, w0lo_early = sem("w0hi_first"), sem("w0lo_first"), sem("w0lo_early")
        mlo_first, mlo_last, xlo_first = sem("mlo_first"), sem("mlo_last"), sem("xlo_first")
        merge_mm, m_done, mhi_done, mlo_done = sem("merge_mm"), sem("m_done"), sem("mhi_done"), sem("mlo_done")
        xhi_done, xlo_done = sem("xhi_done"), sem("xlo_done")
        apply_mm = sem("apply_mm")
        out_done = [sem(f"out_done{j}") for j in range(NT)]
        last_done = sem("last_done")
        stored = [[sem(f"stored{i}{j}") for j in range(NT)] for i in range(2)]

        block = ctx.enter_context(nc.Block())

        @block.sync
        def _(sp):
            def load_pack(q):
                at = MIXW + q * PACKW
                sp.dma_start(packs_sb[:, at:at + PACKW], packs[:, at:at + PACKW]).then_inc(pack_in[q], 16)

            head = MIXW + C
            sp.dma_start(packs_sb[:, 0:head], packs[:, 0:head]).then_inc(mix_in, 16)
            sp.dma_start(packs_sb[:, head:MIXW + PACKW], packs[:, head:MIXW + PACKW]).then_inc(pack_in[0], 16)
            load_pack(1)
            sp.dma_start(lora_sb[:, :], lora_in).then_inc(lora_arrived, 16)
            load_pack(2)
            sp.dma_start(base_sb[:, :, :], base.rearrange("p (j o) -> p j o", j=NT)).then_inc(base_in, 16)
            for q in range(3, NQ):
                load_pack(q)
            for b in range(NB):
                sp.dma_start(x_sb[:, b], xT[b].rearrange("p (j n) -> p j n", j=NT)).then_inc(x_in[b], 16)
                if b == 0:
                    sp.dma_start(rows_sb[:, :, :], rows.rearrange("p (j c) -> p j c", j=NT + 1)).then_inc(rows_in, 16)
            for b in range(NB):
                for j in range(NT):
                    if b < NB - 1 or j < NT - 1:
                        sp.wait_ge(out_done[j], b + 1)
                        sp.dma_start(outT[b, j], out_sb[:, b % 2, j, :]).then_inc(stored[b % 2][j], 16)
            sp.wait_ge(last_done, 1)
            sp.dma_start(outT[NB - 1, 1, :, 0:TOK // 2],
                         out_sb[:, 1, 1, 0:TOK // 2]).then_inc(stored[1][1], 16)
            sp.wait_ge(out_done[1], NB)
            sp.dma_start(outT[NB - 1, 1, :, TOK // 2:TOK],
                         out_sb[:, 1, 1, TOK // 2:TOK]).then_inc(stored[1][1], 16)
            for i in range(2):
                for j in range(NT):
                    sp.wait_ge(stored[i][j], 16 * (NB // 2 + (i == 1 and j == 1)))

        @block.gpsimd
        def _(pool):
            pool.memset(ident[:, :], 0.0).then_inc(ident_zero, 1)
            pool.wait_ge(ident_zero, 1)
            pool.affine_select(out=ident[:, :], in_=ident[:, :], compare_op=ALU.not_equal, fill=1.0,
                               base=0, pattern=[[-1, P]], channel_multiplier=1).then_inc(ident_done, 1)
            pool.wait_ge(ident_done, 1)
            pool.wait_ge(base_in, 16)
            for j in range(NT):
                diag = base_sb[:, j, j * P:(j + 1) * P]
                pool.tensor_tensor(diag, diag, ident[:, :], ALU.add).then_inc(base_done, 1)

            def w1_lo(b):
                pool.wait_ge(w1hi_done, b + 1)
                if b >= W1BUF:
                    pool.wait_ge(merge_mm, b - W1BUF + 1)
                pool.tensor_tensor(W1_lo[:, b % W1BUF], W1[:, b % W1BUF], W1_hi[:, b % W1BUF].bitcast(f32),
                                   ALU.subtract).then_inc(w1lo_done, 1)

            def w0_lo(b):
                pool.wait_ge(w0hi_done, b + 1)
                if b >= 2:
                    pool.wait_ge(merge_mm, b - 1)
                pool.tensor_tensor(W0_lo[:, b % 2], W0[:, b], W0_hi[:, b % 2].bitcast(f32),
                                   ALU.subtract).then_inc(w0lo_done, 1)

            def m_lo(b):
                pool.wait_ge(mhi_done, b + 1)
                if b >= 2:
                    pool.wait_ge(apply_mm, 2 * (b - 1))
                pool.tensor_tensor(M_lo[:, b % 2], M[:, b % 2], M_hi[:, b % 2].bitcast(f32),
                                   ALU.subtract).then_inc(mlo_done, 1)

            w1_lo(0)
            w1_lo(1)
            pool.wait_ge(w0hi_first, 1)
            pool.tensor_tensor(W0_lo[:, 0, :, 0:H], W0[:, 0, :, 0:H], W0_hi[:, 0, :, 0:H].bitcast(f32),
                               ALU.subtract).then_inc(w0lo_first, 1)
            pool.wait_ge(xhi_done, 1)
            pool.tensor_tensor(x_lo[:, 0], x_sb[:, 0], x_hi[:, 0].bitcast(f32), ALU.subtract).then_inc(xlo_first, 1)
            w1_lo(2)
            for b in range(NB):
                if b + 2 < NB:
                    w0_lo(b + 2)
                if b + 1 < NB - 1:
                    m_lo(b + 1)
                if b + 3 < NB:
                    w1_lo(b + 3)

        @block.scalar
        def _(act):
            def a_hi(b):
                nc.scalar.activation(A_hi[:, b], A_er, ACT.Copy,
                                     scale=cond_er[:, b:b + 1]).then_inc(ahi_done, 1)

            def w1_hi(b):
                act.wait_ge(w1_done, b + 1)
                if b >= W1BUF:
                    act.wait_ge(merge_mm, b - W1BUF + 1)
                nc.scalar.activation(W1_hi[:, b % W1BUF], W1[:, b % W1BUF], ACT.Copy).then_inc(w1hi_done, 1)

            def w0_hi(b):
                if b >= 2:
                    act.wait_ge(merge_mm, b - 1)
                nc.scalar.activation(W0_hi[:, b % 2], W0[:, b], ACT.Copy).then_inc(w0hi_done, 1)

            def m_hi(b):
                act.wait_ge(m_done, b + 1)
                if b >= 2:
                    act.wait_ge(apply_mm, 2 * (b - 1))
                nc.scalar.activation(M_hi[:, b % 2], M[:, b % 2], ACT.Copy).then_inc(mhi_done, 1)

            def split_x_hi(b):
                act.wait_ge(x_in[b], 16)
                if b >= XBUF:
                    act.wait_ge(apply_mm, 2 * (b - XBUF + 1))
                nc.scalar.activation(x_hi[:, b % XBUF], x_sb[:, b], ACT.Copy).then_inc(xhi_done, 1)

            def out0(b):
                act.wait_ge(apply_mm, 2 * b + 1)
                if b == 0:
                    act.wait_ge(bias_done, 1)
                if b >= 2:
                    act.wait_ge(stored[b % 2][0], 16 * (b // 2))
                nc.scalar.activation(out_sb[:, b % 2, 0, :], ps_out[b % 2 * NT][:, :], ACT.Identity,
                                     bias=bias_sb[:, 0, b:b + 1]).then_inc(out_done[0], 1)

            act.wait_ge(lora_arrived, 16)
            a_hi(0)
            nc.scalar.activation(B_hi[:, :], B_er, ACT.Copy, scale=SCALING).then_inc(bhi_done, 1)
            for b in range(1, EARLY):
                a_hi(b)
            w1_hi(0)
            w1_hi(1)
            act.wait_ge(w0_done, NQ // 2)
            nc.scalar.activation(W0_hi[:, 0, :, 0:H], W0[:, 0, :, 0:H], ACT.Copy).then_inc(w0hi_first, 1)
            split_x_hi(0)
            w1_hi(2)
            act.wait_ge(w0_done, NQ)
            nc.scalar.activation(W0_hi[:, 0, :, H:C], W0[:, 0, :, H:C], ACT.Copy).then_inc(w0hi_done, 1)
            w0_hi(1)
            m_hi(0)
            w0_hi(2)
            split_x_hi(1)
            for b in range(NB):
                if b + 1 < NB:
                    m_hi(b + 1)
                if EARLY <= b + 5 < NB:
                    a_hi(b + 5)
                if b == 0:
                    w1_hi(3)
                if b + 2 < NB:
                    split_x_hi(b + 2)
                out0(b)
                if 4 <= b + 3 < NB:
                    w1_hi(b + 3)
                if b + 3 < NB:
                    w0_hi(b + 3)
            b = NB - 1
            act.wait_ge(apply_mm, 2 * b + 2)
            act.wait_ge(stored[b % 2][1], 16 * (b // 2))
            nc.scalar.activation(out_sb[:, b % 2, 1, 0:TOK // 2], ps_out[b % 2 * NT + 1][:, 0:TOK // 2], ACT.Identity,
                                 bias=bias_sb[:, 1, b:b + 1]).then_inc(last_done, 1)

        @block.vector
        def _(dve):
            nc.vector.memset(warm[:, :], 0.0).then_inc(warm_set, 1)

            def a_lo(b):
                dve.wait_ge(ahi_done, b + 1)
                nc.vector.scalar_tensor_tensor(out=A_lo[:, b], in0=A_er, scalar=cond_er[:, b:b + 1],
                                               in1=A_hi[:, b].bitcast(f32),
                                               op0=ALU.mult, op1=ALU.subtract).then_inc(alo_done, 1)

            def w1(b):
                dve.wait_ge(lora_mm, b + 1)
                if b >= W1BUF:
                    dve.wait_ge(m_done, b - W1BUF + 1)
                    dve.wait_ge(w1lo_done, b - W1BUF + 1)
                nc.vector.tensor_tensor(W1[:, b % W1BUF], ps_lora[b % 2][:, :, :], base_sb[:, :, :],
                                        ALU.add).then_inc(w1_done, 1)

            def w0(q):
                dve.wait_ge(mix_mm, q + 1)
                dve.wait_ge(pack_in[q], 16)
                ts = slice(q * TQ, (q + 1) * TQ)
                nc.vector.tensor_tensor(
                    W0[:, :, :, ts].rearrange("p b j t -> p j b t"),
                    ps_mix[q % 4][:, :].rearrange("p (j b t) -> p j b t", j=NT, t=TQ),
                    pack(q)[1].unsqueeze(2).to_broadcast([P, NT, NB, TQ]),
                    ALU.mult).then_inc(w0_done, 1)

            def split_x_lo(b):
                dve.wait_ge(xhi_done, b + 1)
                if b >= XBUF:
                    dve.wait_ge(apply_mm, 2 * (b - XBUF + 1))
                nc.vector.tensor_tensor(x_lo[:, b % XBUF], x_sb[:, b], x_hi[:, b % XBUF].bitcast(f32),
                                        ALU.subtract).then_inc(xlo_done, 1)

            def m(b):
                dve.wait_ge(merge_mm, b + 1)
                if b == 2:
                    dve.wait_ge(mlo_first, 1)
                if b >= 3:
                    dve.wait_ge(mlo_done, b - 2)
                nc.vector.tensor_tensor(M[:, b % 2], ps_merge[b % 2][:, :, :], W1[:, b % W1BUF],
                                        ALU.add).then_inc(m_done, 1)

            def out1(b):
                dve.wait_ge(apply_mm, 2 * b + 2)
                if b >= 2:
                    dve.wait_ge(stored[b % 2][1], 16 * (b // 2))
                nc.vector.tensor_scalar(out_sb[:, b % 2, 1, :], ps_out[b % 2 * NT + 1][:, :],
                                        bias_sb[:, 1, b:b + 1], None, ALU.add).then_inc(out_done[1], 1)

            def dot(row, out):
                return nc.vector.tensor_tensor_reduce(out=row_products[:, :], in0=row, in1=bias0_row, scale=1.0,
                                                      scalar=0.0, op0=ALU.mult, op1=ALU.add, accum_out=out)

            dve.wait_ge(lora_arrived, 16)
            a_lo(0)
            dve.wait_ge(bhi_done, 1)
            nc.vector.scalar_tensor_tensor(out=B_lo[:, :], in0=B_er, scalar=SCALING, in1=B_hi[:, :].bitcast(f32),
                                           op0=ALU.mult, op1=ALU.subtract).then_inc(blo_done, 1)
            a_lo(1)
            w0(0)
            a_lo(2)
            w0(1)
            dve.wait_ge(base_done, NT)
            w1(0)
            a_lo(3)
            w0(2)
            w1(1)
            w0(3)
            w0(4)
            a_lo(4)
            w1(2)
            w0(5)
            w0(6)
            w0(7)
            dve.wait_ge(rows_in, 16)
            dot(A_er, A_bias0[:, :]).then_inc(dots_done, 1)
            dve.wait_ge(dots_done, 1)
            nc.vector.tensor_scalar(low_bias[:, :], cond_er, A_bias0[:, :], SCALING,
                                    ALU.mult, ALU.mult).then_inc(low_done, 1)
            dve.wait_ge(w0hi_done, 1)
            nc.vector.tensor_tensor(W0_lo[:, 0, :, H:C], W0[:, 0, :, H:C], W0_hi[:, 0, :, H:C].bitcast(f32),
                                    ALU.subtract).then_inc(w0lo_early, 1)
            dve.wait_ge(w0hi_done, 2)
            nc.vector.tensor_tensor(W0_lo[:, 1], W0[:, 1], W0_hi[:, 1].bitcast(f32), ALU.subtract).then_inc(w0lo_early, 1)
            m(0)
            dve.wait_ge(mhi_done, 1)
            nc.vector.tensor_tensor(M_lo[:, 0], M[:, 0], M_hi[:, 0].bitcast(f32), ALU.subtract).then_inc(mlo_first, 1)
            m(1)
            w1(3)
            split_x_lo(1)
            for j in range(NT):
                dve.wait_ge(dots_done, 1 + j)
                dot(base_rows[:, j, :], base_bias0[:, j:j + 1]).then_inc(dots_done, 1)
            nc.vector.tensor_tensor(bias_sum[:, :], bias0, bias1, ALU.add).then_inc(fixed_done, 1)
            dve.wait_ge(fixed_done, 1)
            dve.wait_ge(dots_done, 1 + NT)
            nc.vector.tensor_tensor(fixed_bias[:, :], bias_sum[:, :], base_bias0[:, :], ALU.add).then_inc(fixed_done, 1)
            dve.wait_ge(fixed_done, 2)
            dve.wait_ge(bias_mm, 1)
            for j in range(NT):
                last = nc.vector.tensor_scalar(bias_sb[:, j, :], ps_bias[:, j, :], fixed_bias[:, j:j + 1], None, ALU.add)
            last.then_inc(bias_done, 1)
            dve.wait_ge(bias_done, 1)
            for b in range(1, NB):
                out1(b - 1)
                if b + 1 < NB:
                    m(b + 1)
                if b + 1 == NB - 1:
                    dve.wait_ge(mhi_done, NB)
                    dve.wait_ge(apply_mm, 2 * (NB - 2))
                    nc.vector.tensor_tensor(M_lo[:, (NB - 1) % 2], M[:, (NB - 1) % 2], M_hi[:, (NB - 1) % 2].bitcast(f32),
                                            ALU.subtract).then_inc(mlo_last, 1)
                if b >= 1 and b + 4 < NB:
                    a_lo(b + 4)
                if b + 1 < NB - 1:
                    split_x_lo(b + 1)
                if b + 2 == NB - 1:
                    split_x_lo(b + 2)
                if b + 3 < NB:
                    w1(b + 3)
            b = NB - 1
            dve.wait_ge(apply_mm, 2 * b + 3)
            dve.wait_ge(stored[b % 2][1], 16 * (b // 2))
            nc.vector.tensor_scalar(out_sb[:, b % 2, 1, TOK // 2:TOK], ps_last,
                                    bias_sb[:, 1, b:b + 1], None, ALU.add).then_inc(out_done[1], 1)

        @block.tensor
        def _(pe):
            def product(out, terms, lo_ready=None):
                for n, (hi_l, _, hi_r, lo_r) in enumerate(terms):
                    nc.tensor.matmul(out, hi_l, hi_r, start=(n == 0), stop=False)
                    nc.tensor.matmul(out, hi_l, lo_r, start=False, stop=False)
                if lo_ready is not None:
                    pe.wait_ge(*lo_ready)
                for n, (_, lo_l, hi_r, _) in enumerate(terms):
                    mm = nc.tensor.matmul(out, lo_l, hi_r, start=False, stop=(n == len(terms) - 1))
                return mm

            def lora(b):
                pe.wait_ge(ahi_done, b + 1)
                if b == 0:
                    pe.wait_ge(blo_done, 1)
                if b >= 2:
                    pe.wait_ge(w1_done, b - 1)
                for j in range(NT):
                    cols = slice(j * P, (j + 1) * P)
                    mm = product(ps_lora[b % 2][:, j, :],
                                 [(A_hi[:, b, cols], A_lo[:, b, cols], B_hi[:, :], B_lo[:, :])],
                                 lo_ready=(alo_done, b + 1))
                mm.then_inc(lora_mm, 1)

            def mixed(q):
                if q == 0:
                    pe.wait_ge(mix_in, 16)
                else:
                    pe.wait_ge(pack_in[q], 16)
                if q >= 4:
                    pe.wait_ge(w0_done, q - 3)
                dst = ps_mix[q % 4][:, :].rearrange("p (j b k t) -> p j b k t", j=NT, k=KQ, t=TB)
                for k in range(KQ):
                    if q == 0 and k == 1:
                        pe.wait_ge(pack_in[0], 16)
                    for j in range(NT):
                        mm = nc.tensor.matmul(dst[:, j, :, k, :], pack(q)[0][:, k, j * P:(j + 1) * P], mix,
                                              start=True, stop=True)
                mm.then_inc(mix_mm, 1)

            def merge_half(b, i, lo_ready):
                rows = slice(i * P, (i + 1) * P)
                return product(ps_merge[b % 2][:, i, :],
                               [(W0_hi[:, b % 2, j, rows], W0_lo[:, b % 2, j, rows],
                                 W1_hi[:, b % W1BUF, j], W1_lo[:, b % W1BUF, j]) for j in range(NT)], lo_ready)

            def merge(b):
                pe.wait_ge(w0hi_done, b + 1)
                pe.wait_ge(w1lo_done, b + 1)
                if b >= 2:
                    pe.wait_ge(m_done, b - 1)
                for i in range(NT):
                    mm = merge_half(b, i, (w0lo_early, 2) if b == 1 else (w0lo_done, b - 1))
                mm.then_inc(merge_mm, 1)

            def apply(b):
                pe.wait_ge(mhi_done, b + 1)
                if b == 0:
                    pe.wait_ge(xlo_first, 1)
                else:
                    pe.wait_ge(xlo_done, b)
                m_lo_ready = (mlo_first, 1) if b == 0 else (mlo_last, 1) if b == NB - 1 else (mlo_done, b)
                for i in range(NT):
                    if b >= 2:
                        pe.wait_ge(out_done[i], b - 1)
                    if b == 1 and i == 1:
                        pe.wait_ge(bias_done, 1)
                    cols = slice(i * P, (i + 1) * P)
                    whole = b < NB - 1 or i < NT - 1
                    for n in [slice(0, TOK)] if whole else [slice(0, TOK // 2), slice(TOK // 2, TOK)]:
                        bank = ps_out[b % 2 * NT + i][:, n] if n.start == 0 else ps_last
                        product(bank, [(M_hi[:, b % 2, j, cols], M_lo[:, b % 2, j, cols],
                                        x_hi[:, b % XBUF, j, n], x_lo[:, b % XBUF, j, n]) for j in range(NT)],
                                m_lo_ready).then_inc(apply_mm, 1)

            pe.wait_ge(warm_set, 1)
            for _ in range(WARM):
                nc.tensor.matmul(ps_merge[0][:, 0, 0:P], warm[:, :], warm[:, :], start=True, stop=True)
            mixed(0)
            mixed(1)
            lora(0)
            mixed(2)
            lora(1)
            mixed(3)
            mixed(4)
            lora(2)
            mixed(5)
            mixed(6)
            mixed(7)
            pe.wait_ge(w0hi_first, 1)
            pe.wait_ge(w1lo_done, 1)
            merge_half(0, 0, (w0lo_first, 1))
            lora(3)
            lora(4)
            pe.wait_ge(w0hi_done, 1)
            merge_half(0, 1, (w0lo_early, 1)).then_inc(merge_mm, 1)
            merge(1)
            pe.wait_ge(w0_done, NQ)
            pe.wait_ge(low_done, 1)
            for i in range(NT):
                mm = nc.tensor.matmul(ps_bias[:, i, :], B_er[:, i * P:(i + 1) * P], low_bias[:, :],
                                      start=True, stop=True)
            mm.then_inc(bias_mm, 1)
            apply(0)
            for b in range(1, NB):
                if b + 1 < NB:
                    merge(b + 1)
                apply(b)
                if b + LEAD < NB:
                    lora(b + LEAD)


def kernel(x, cond_8, L0_cond_weight, L0_cond_mask, L0_cond_bias,
           L1_cond_W_base, L1_cond_b_base, L1_cond_As, L1_cond_Bs):
    import numpy as np
    import concourse.bacc as bacc
    from concourse.bass_utils import run_bass_kernel_spmd

    P = 128
    x, cond, weight, mask, bias0, base, bias1, As, Bs = (
        np.asarray(a) for a in (x, cond_8, L0_cond_weight, L0_cond_mask, L0_cond_bias,
                                L1_cond_W_base, L1_cond_b_base, L1_cond_As, L1_cond_Bs))
    NB, TOK, C = x.shape
    G = weight.shape[0]
    NT = C // P
    TB = P // G
    R = As.shape[1]

    def halves(a):
        return np.ascontiguousarray(a.reshape(NT, P, -1).transpose(1, 0, 2).reshape(P, -1))

    KQ = 2
    TQ = KQ * TB
    NQ = C // TQ
    mix = np.zeros((G, TB, NB, TB), cond.dtype)
    for t in range(TB):
        mix[:, t, :, t] = cond.T
    experts = weight.reshape(G, C, NQ, KQ, TB).transpose(0, 4, 2, 3, 1).reshape(P, NQ, KQ * C)
    masks = mask.reshape(NT, P, NQ, TQ).transpose(1, 2, 0, 3).reshape(P, NQ, NT * TQ)
    packs = np.concatenate([mix.reshape(P, P), np.concatenate([experts, masks], axis=2).reshape(P, -1)], axis=1)
    A_er = As.reshape(G * R, C)
    lora = np.concatenate([np.repeat(cond.T, R, axis=0), halves(bias0[:, None]), halves(bias1[:, None]),
                           A_er, Bs.transpose(0, 2, 1).reshape(G * R, C)], axis=1)
    rows = np.concatenate([halves(base), np.broadcast_to(bias0, (P, C))], axis=1)
    xT = np.ascontiguousarray(x.transpose(0, 2, 1).reshape(NB, NT, P, TOK).transpose(0, 2, 1, 3).reshape(NB, P, NT * TOK))
    arrays = {"packs": packs, "lora": lora, "base": halves(base.T), "rows": rows, "xT": xT}
    arrays = {n: np.ascontiguousarray(a) for n, a in arrays.items()}

    nc = bacc.Bacc("TRN2", target_bir_lowering=False, num_devices=1)
    f32 = mybir.dt.float32
    args = [nc.dram_tensor(f"{n}_dram", a.shape, f32, kind="ExternalInput").ap() for n, a in arrays.items()]
    outT = nc.dram_tensor("outT_dram", (NB, NT, P, TOK), f32, kind="ExternalOutput").ap()
    conditional_residual_kernel(nc, *args, outT)
    r = run_bass_kernel_spmd(nc, [{f"{n}_dram": a for n, a in arrays.items()}], core_ids=[0])
    got = np.asarray(r.results[0]["outT_dram"])
    return np.ascontiguousarray(got.reshape(NB, C, TOK).transpose(0, 2, 1))
```
